# Optimizing a Trainium2 kernel written in Bass

```python
import numpy as np
import jax
import jax.numpy as jnp

def _softmax(x, axis=-1):
    return jax.nn.softmax(x, axis=axis)

def _gelu(x):
    return jax.nn.gelu(x, approximate=True)

def _silu(x):
    return jax.nn.silu(x)

def _sigmoid(x):
    return jax.nn.sigmoid(x)

def _layernorm(x, axis=-1, eps=1e-05):
    m = jnp.mean(x, axis=axis, keepdims=True)
    v = jnp.var(x, axis=axis, keepdims=True)
    return (x - m) / jnp.sqrt(v + eps)

def _scatter_add(tgt, idx, src, axis=0):
    return tgt.at[idx].add(src)

def _segment_sum(src, seg, n):
    return jax.ops.segment_sum(src, seg, n)
kernel_name = 'mk_adj_resnorm_d2_adj_r2_8b3180'

def setup_inputs(seed: int=0):
    np.random.seed(seed)
    _w = jnp.asarray

    def _rec_inputs():
        import jax
        import jax.numpy as jnp
        _gk = jax.random.key(seed)
        x = -0.0002928 + 1 * jax.random.normal(jax.random.fold_in(_gk, 1), (64, 128, 256), jnp.float32)
        _w = (1.0 + jnp.arange(128, dtype=jnp.float32)) ** (-0.5)
        _w = _w / _w.mean()
        _pij = jnp.clip(0.0625 * _w[:, None] * _w[None, :], 0.0, 1.0)
        _a = jax.random.uniform(jax.random.fold_in(_gk, 2), (64, 128, 128)) < _pij
        _a = jnp.logical_or(_a, jnp.swapaxes(_a, -1, -2))
        _a = jnp.logical_or(_a, jnp.eye(128, dtype=bool))
        _af = _a.astype(jnp.float32)
        _af = _af * jax.random.uniform(jax.random.fold_in(_gk, 3), (64, 128, 128), jnp.float32, 0.05, 1)
        adj = _af
        return (x, adj)
    x, adj = _rec_inputs()

    def _L0_gnn_setup():
        import jax, jax.numpy as jnp
        import numpy as np
        B, N, DIN, DOUT, K = (4, 1024, 256, 256, 3)
        key = jax.random.key(seed)
        ks = jax.random.split(key, 8)
        X = jax.random.normal(ks[0], (B, N, DIN), dtype=jnp.float32)
        A = jax.random.uniform(ks[1], (B, N, N), dtype=jnp.float32)
        Wv = jax.random.normal(ks[2], (DIN, DOUT), dtype=jnp.float32) * 0.02
        bv = jax.random.normal(ks[3], (DOUT,), dtype=jnp.float32) * 0.02
        aw = jax.random.normal(ks[4], (2 * DOUT, 1), dtype=jnp.float32) * 0.05
        ab = jax.random.normal(ks[5], (1,), dtype=jnp.float32) * 0.05
        Wk = jax.random.normal(ks[6], (K, DIN, DOUT), dtype=jnp.float32) * 0.02
        bk = jax.random.normal(ks[7], (K, DOUT), dtype=jnp.float32) * 0.02
        return {'X': X, 'A': A, 'Wv': Wv, 'bv': bv, 'aw': aw, 'ab': ab, 'Wk': Wk, 'bk': bk}
    _L0_gnn_all = _L0_gnn_setup()
    _L0_gnn_in = {k: v for k, v in _L0_gnn_all.items() if k in ('Wv', 'bv', 'aw', 'ab', 'Wk', 'bk')}
    del _L0_gnn_all

    def _L1_gnn_setup():
        import jax, jax.numpy as jnp
        import numpy as np
        key = jax.random.key(seed)
        k1, k2, k3 = jax.random.split(key, 3)
        B, N, F_in, F_out = (64, 62, 256, 256)
        x = jax.random.normal(k1, (B, N, F_in), dtype=jnp.float32)
        adj = jax.random.uniform(k2, (B, N, N), dtype=jnp.float32)
        std = (2.0 / (F_in + F_out)) ** 0.5
        w = jax.random.normal(k3, (F_in, F_out), dtype=jnp.float32) * std
        return {'x': x, 'adj': adj, 'w': w}
    _L1_gnn_all = _L1_gnn_setup()
    _L1_gnn_in = {k: v for k, v in _L1_gnn_all.items() if k in ('w',)}
    del _L1_gnn_all
    return {'x': x, 'adj': adj, 'L0_gnn_Wv': _L0_gnn_in['Wv'], 'L0_gnn_bv': _L0_gnn_in['bv'], 'L0_gnn_aw': _L0_gnn_in['aw'], 'L0_gnn_ab': _L0_gnn_in['ab'], 'L0_gnn_Wk': _L0_gnn_in['Wk'], 'L0_gnn_bk': _L0_gnn_in['bk'], 'L1_gnn_w': _L1_gnn_in['w']}

def reference(x, adj, L0_gnn_Wv, L0_gnn_bv, L0_gnn_aw, L0_gnn_ab, L0_gnn_Wk, L0_gnn_bk, L1_gnn_w):
    import jax
    import jax.numpy as jnp

    def _L0_gnn_ref(X, A, Wv, bv, aw, ab, Wk, bk):
        import jax, jax.numpy as jnp
        import numpy as np
        B, N, DIN, DOUT, K = (4, 1024, 256, 256, 3)
        d = Wv.shape[1]
        Xw = X @ Wv + bv
        sj = Xw @ aw[:d, 0]
        si = Xw @ aw[d:, 0]
        e = jax.nn.leaky_relu(sj[:, None, :] + si[:, :, None] + ab[0], negative_slope=0.2)
        alpha_matrix = A * jnp.exp(e)
        transition = alpha_matrix / (jnp.sum(alpha_matrix, axis=-1, keepdims=True) + 1e-12)
        H = jnp.zeros(X.shape[:-1] + (d,), dtype=X.dtype)
        Xk = X
        for k in range(Wk.shape[0]):
            H = H + Xk @ Wk[k] + bk[k]
            Xk = jnp.einsum('bij,bjd->bid', transition, Xk)
        return jax.nn.relu(H)

    def _L1_gnn_ref(x, adj, w):
        import jax, jax.numpy as jnp
        import numpy as np
        agg = jnp.einsum('bnm,bmf->bnf', adj, x)
        return jnp.einsum('bnf,fo->bno', agg, w)
    x = _layernorm(x + _L0_gnn_ref(x, adj, L0_gnn_Wv, L0_gnn_bv, L0_gnn_aw, L0_gnn_ab, L0_gnn_Wk, L0_gnn_bk), axis=-1)
    x = _layernorm(x + _L1_gnn_ref(x, adj, L1_gnn_w), axis=-1)
    return x

_drawn_inputs = setup_inputs


def setup_inputs(seed=0):
    import zlib

    import numpy as np

    out = dict(_drawn_inputs(seed))
    spreads = {}
    factors = {'L0_gnn_Wv': 2.962, 'L0_gnn_bv': 8.0, 'L0_gnn_aw': 3.042}
    for name, (base, spread) in spreads.items():
        noise = np.random.default_rng([zlib.crc32(name.encode()), seed]).standard_normal(out[name].shape)
        drawn = base * np.exp(spread * noise) if base else spread * noise
        out[name] = jnp.asarray(drawn.astype(out[name].dtype))
    for name, factor in factors.items():
        out[name] = (out[name] * factor).astype(out[name].dtype)
    return out
```

```python
from contextlib import ExitStack

import concourse.bass as bass
from concourse import mybir

F32 = mybir.dt.float32
F32R = mybir.dt.float32r
ALU = mybir.AluOpType
ACT = mybir.ActivationFunctionType

P = 128
PER = 2
DMA = 16
SLOPE = 0.2
ROWSUM_EPS = 1e-12
NORM_EPS = 1e-5


def resnorm_graph_kernel(nc, packed, nodes, Wv, bv, aw, ab, Wk, bk, w, out):
    PAIRS = nodes.shape[0]
    D = Wv.shape[0]
    C = D // P
    HOPS = Wk.shape[0]
    XT, AN, AT = 0, C * PER * P, C * PER * P + PER * P
    IN_COLS = AT + PER * P
    FIRST, LOOPED = 4, PAIRS - 8
    assert (P, C, HOPS) == (nodes.shape[1], 2, 3) and LOOPED % 2 == 0

    with ExitStack() as ctx:
        def sb(name, shape, dt=F32):
            return ctx.enter_context(nc.sbuf_tensor(name, shape, dt))

        def ps(name, shape):
            return ctx.enter_context(nc.psum_tensor(name, shape, F32))

        def sem(name):
            return ctx.enter_context(nc.semaphore(name))

        packed_sb = [sb(f"packed{s}", [P, IN_COLS]) for s in range(2)]
        nodes_sb = [sb(f"nodes{s}", [P, PER, D]) for s in range(2)]
        Wk_sb = sb("Wk_sb", [P, HOPS, C, D])
        Wv_sb = sb("Wv_sb", [P, C, D])
        w_sb = sb("w_sb", [P, C, D])
        aw_rows = sb("aw_rows", [P, 2 * D])
        bv_rows = sb("bv_rows", [P, D])
        ab_col = sb("ab_col", [P, 1])
        products = sb("products", [P, D])
        u = sb("u", [P, C, 2])
        shift = sb("shift", [P, 4])
        WX_hi, WX_lo = sb("WX_hi", [P, C, 2, D], F32R), sb("WX_lo", [P, C, 2, D], F32R)
        WY_hi, WY_lo = sb("WY_hi", [P, C, D + 2], F32R), sb("WY_lo", [P, C, D + 2], F32R)
        w_hi, w_lo = sb("w_hi", [P, C, D], F32R), sb("w_lo", [P, C, D], F32R)
        bias_in = sb("bias_in", [P, D])
        bias_parts = sb("bias_parts", [P, D], F32R)
        bias_tmp = sb("bias_tmp", [P, D], F32R)
        ones = sb("ones", [P, P], F32R)
        identity = sb("identity", [P, P])
        minus_half = sb("minus_half", [P, PER])
        epsilon = sb("epsilon", [P, PER])
        XT_hi = [sb(f"XT_hi{s}", [P, C, PER, P], F32R) for s in range(2)]
        XT_lo = [sb(f"XT_lo{s}", [P, C, PER, P], F32R) for s in range(2)]
        AT_hi = [sb(f"AT_hi{s}", [P, PER, P], F32R) for s in range(2)]
        AT_lo = [sb(f"AT_lo{s}", [P, PER, P], F32R) for s in range(2)]
        V2_hi, V2_lo = sb("V2_hi", [P, PER, D], F32R), sb("V2_lo", [P, PER, D], F32R)
        V1_hi, V1_lo = sb("V1_hi", [P, PER, D], F32R), sb("V1_lo", [P, PER, D], F32R)
        TT_hi, TT_lo = sb("TT_hi", [P, PER, P], F32R), sb("TT_lo", [P, PER, P], F32R)
        y_hi, y_lo = sb("y_hi", [P, PER, D], F32R), sb("y_lo", [P, PER, D], F32R)
        agg_hi, agg_lo = sb("agg_hi", [P, C, PER, P], F32R), sb("agg_lo", [P, C, PER, P], F32R)
        scores = sb("scores", [P, PER, 2])
        sums = sb("sums", [P, PER, P])
        leaky = sb("leaky", [P, PER, P])
        expd = sb("expd", [P, PER, P])
        alpha = sb("alpha", [P, PER, P])
        rowsum = sb("rowsum", [P, PER])
        rowsum_eps = sb("rowsum_eps", [P, PER])
        inv_rowsum = sb("inv_rowsum", [P, PER])
        T = sb("T", [P, PER, P])
        res1 = sb("res1", [P, PER, D])
        y = [sb(f"y{s}", [P, PER, D]) for s in range(2)]
        res2 = sb("res2", [P, PER, D])
        out_sb = [sb(f"out_sb{s}", [P, PER, D]) for s in range(2)]
        stats1, stats2 = sb("stats1", [P, PER, 6]), sb("stats2", [P, PER, 6])
        moments1, moments2 = sb("moments1", [P, PER, 2]), sb("moments2", [P, PER, 2])
        var1, var2 = sb("var1", [P, PER]), sb("var2", [P, PER])
        rstd1, rstd2 = sb("rstd1", [P, PER]), sb("rstd2", [P, PER])

        ps_x = ps("ps_x", [P, PER, 512])
        ps_y = ps("ps_y", [P, PER, 512])
        ps_s = ps("ps_s", [P, 4, P])
        ps_t = ps("ps_t", [P, 4, P])
        ps_agg = ps("ps_agg", [P, C, PER, P])
        ps_out = ps("ps_out", [P, PER, D])

        packed_loaded = [sem(f"packed_loaded{s}") for s in range(2)]
        nodes_loaded = [sem(f"nodes_loaded{s}") for s in range(2)]
        stored = [sem(f"stored{s}") for s in range(2)]
        score_weights_loaded = sem("score_weights_loaded")
        Wk_loaded = sem("Wk_loaded")
        w_loaded = sem("w_loaded")
        bias_loaded = sem("bias_loaded")
        bias_cleared = sem("bias_cleared")
        dve_setup = sem("dve_setup")
        shift_ready = sem("shift_ready")
        WY_ready = sem("WY_ready")
        WX_ready = sem("WX_ready")
        w_ready = sem("w_ready")
        pool_setup = sem("pool_setup")
        pool_chain = sem("pool_chain")
        identity_ready = sem("identity_ready")
        y_done = sem("y_done")
        spread_done = sem("spread_done")
        v1_done = sem("v1_done")
        h_done = sem("h_done")
        tt_done = sem("tt_done")
        agg_done = sem("agg_done")
        out_done = sem("out_done")
        scores_ready = sem("scores_ready")
        v2_hi_ready = sem("v2_hi_ready")
        v1_hi_ready = sem("v1_hi_ready")
        sums_ready = sem("sums_ready")
        exp_ready = sem("exp_ready")
        agg_hi_ready = sem("agg_hi_ready")
        xt_hi_ready = sem("xt_hi_ready")
        at_hi_ready = sem("at_hi_ready")
        tt_hi_ready = sem("tt_hi_ready")
        y_hi_ready = sem("y_hi_ready")
        v1_lo_ready = sem("v1_lo_ready")
        res1_ready = sem("res1_ready")
        leaky_ready = sem("leaky_ready")
        stats1_ready = sem("stats1_ready")
        moments1_ready = sem("moments1_ready")
        agg_lo_ready = sem("agg_lo_ready")
        alpha_ready = sem("alpha_ready")
        rowsum_ready = sem("rowsum_ready")
        inv_ready = sem("inv_ready")
        t_ready = sem("t_ready")
        out_ready = sem("out_ready")
        v2_lo_ready = sem("v2_lo_ready")
        y_ready = sem("y_ready")
        tt_lo_ready = sem("tt_lo_ready")
        res2_ready = sem("res2_ready")
        stats2_ready = sem("stats2_ready")
        moments2_ready = sem("moments2_ready")
        var1_ready = sem("var1_ready")
        rstd1_ready = sem("rstd1_ready")
        xt_lo_ready = sem("xt_lo_ready")
        at_lo_ready = sem("at_lo_ready")
        y_lo_ready = sem("y_lo_ready")
        var2_ready = sem("var2_ready")
        rstd2_ready = sem("rstd2_ready")

        def there(i, k):
            return not isinstance(i, int) or 0 <= k < PAIRS

        def loads(i, k):
            return DMA * i + DMA * (k // 2 + 1)

        def all_steps(engine, step):
            for k in range(-2, FIRST):
                step(0, k)
            with engine.Fori(0, LOOPED // 2) as i:
                step(i, FIRST)
                step(i, FIRST + 1)
            for k in range(FIRST + LOOPED, PAIRS + 2):
                step(0, k)

        block = ctx.enter_context(nc.Block())

        @block.sync
        def _(sp):
            def load_packed(i, k):
                if k >= 2:
                    sp.wait_ge(xt_lo_ready, 2 * i + k - 1)
                    sp.wait_ge(at_lo_ready, 2 * i + k - 1)
                    sp.wait_ge(alpha_ready, 2 * i + k - 1)
                sp.dma_start(packed_sb[k % 2][:], packed[2 * i + k]).then_inc(packed_loaded[k % 2], DMA)

            def load_nodes(i, k):
                if k >= 2:
                    sp.wait_ge(res1_ready, 2 * i + k - 1)
                sp.dma_start(nodes_sb[k % 2][:].rearrange("p b d -> p (b d)"),
                             nodes[2 * i + k]).then_inc(nodes_loaded[k % 2], DMA)

            def store(i, k):
                sp.wait_ge(out_ready, 2 * i + k + 1)
                sp.dma_start(out[2 * i + k],
                             out_sb[k % 2][:].rearrange("p b d -> p (b d)")).then_inc(stored[k % 2], DMA)

            load_packed(0, 0)
            sp.dma_start(Wv_sb[:], Wv.rearrange("(c p) n -> p c n", p=P)).then_inc(score_weights_loaded, DMA)
            sp.dma_start(Wk_sb[:, 2], Wk[2].rearrange("(c p) n -> p c n", p=P)).then_inc(Wk_loaded, DMA)
            sp.dma_start(Wk_sb[:, 0], Wk[0].rearrange("(c p) n -> p c n", p=P)).then_inc(Wk_loaded, DMA)
            sp.dma_start(Wk_sb[:, 1], Wk[1].rearrange("(c p) n -> p c n", p=P)).then_inc(Wk_loaded, DMA)
            load_packed(0, 1)
            load_nodes(0, 0)
            sp.dma_start(w_sb[:], w.rearrange("(c p) n -> p c n", p=P)).then_inc(w_loaded, DMA)
            load_nodes(0, 1)

            def step(i, k):
                if k >= 0 and there(i, k + 2):
                    load_nodes(i, k + 2)
                if k >= -1 and there(i, k + 3):
                    load_packed(i, k + 3)
                if there(i, k - 2):
                    store(i, k - 2)

            all_steps(sp, step)
            for s in range(2):
                sp.wait_ge(stored[s], DMA * PAIRS // 2)

        @block.scalar
        def _(act):
            act.dma_start(aw_rows[:], aw.partition_broadcast(P)).then_inc(score_weights_loaded, DMA)
            act.dma_start(bv_rows[:], bv.partition_broadcast(P)).then_inc(score_weights_loaded, DMA)
            act.dma_start(ab_col[:], ab.partition_broadcast(P)).then_inc(score_weights_loaded, DMA)
            act.wait_ge(bias_cleared, 1)
            act.dma_start(bias_in[0:HOPS], bk).then_inc(bias_loaded, DMA)
            act.dma_start(bias_in[32:32 + HOPS], bk).then_inc(bias_loaded, DMA)

            def v1_hi(i, k):
                act.wait_ge(v1_done, 2 * i + k + 1)
                act.activation(V1_hi[:], ps_x[:, :, D:2 * D], ACT.Copy).then_inc(v1_hi_ready, 1)

            def scores_and_v2_hi(i, k):
                act.wait_ge(y_done, 2 * i + k + 1)
                if k == 0:
                    act.wait_ge(shift_ready, 1)
                act.activation(scores[:], ps_y[:, :, D:D + 2], ACT.Identity,
                               bias=shift[:, 3:4]).then_inc(scores_ready, 1)
                act.activation(V2_hi[:], ps_y[:, :, 0:D], ACT.Copy).then_inc(v2_hi_ready, 1)

            def sum_scores(i, k):
                act.wait_ge(scores_ready, 2 * i + k + 1)
                act.wait_ge(spread_done, 2 * i + k + 1)
                for b in range(PER):
                    last = act.activation(sums[:, b], ps_s[:, b], ACT.Identity, bias=scores[:, b, 1:2])
                last.then_inc(sums_ready, 1)

            def exponentials(i, k):
                act.wait_ge(leaky_ready, 2 * i + k + 1)
                act.activation(expd[:], leaky[:], ACT.Exp).then_inc(exp_ready, 1)

            def aggregate_hi(i, k):
                act.wait_ge(agg_done, 2 * i + k + 1)
                act.activation(agg_hi[:], ps_agg[:], ACT.Copy).then_inc(agg_hi_ready, 1)

            def xt_hi(i, k):
                act.wait_ge(packed_loaded[k % 2], loads(i, k))
                act.activation(XT_hi[k % 2][:].rearrange("p c b i -> p (c b i)"),
                               packed_sb[k % 2][:, XT:AN], ACT.Copy).then_inc(xt_hi_ready, 1)

            def at_hi(i, k):
                act.activation(AT_hi[k % 2][:].rearrange("p b i -> p (b i)"),
                               packed_sb[k % 2][:, AT:IN_COLS], ACT.Copy).then_inc(at_hi_ready, 1)

            def tt_hi(i, k):
                act.wait_ge(tt_done, 2 * i + k + 1)
                act.activation(TT_hi[:], ps_t[:, 0:PER], ACT.Copy).then_inc(tt_hi_ready, 1)

            def y_hi_part(i, k):
                act.wait_ge(y_ready, 2 * i + k + 1)
                act.activation(y_hi[:], y[k % 2][:], ACT.Copy).then_inc(y_hi_ready, 1)

            def step(i, k):
                if there(i, k):
                    v1_hi(i, k)
                if there(i, k + 1):
                    scores_and_v2_hi(i, k + 1)
                    sum_scores(i, k + 1)
                    exponentials(i, k + 1)
                if there(i, k - 1):
                    aggregate_hi(i, k - 1)
                if there(i, k + 2):
                    xt_hi(i, k + 2)
                if there(i, k + 1):
                    at_hi(i, k + 1)
                    tt_hi(i, k + 1)
                if there(i, k):
                    y_hi_part(i, k)

            all_steps(act, step)

        @block.vector
        def _(dve):
            setup = [0]

            def then(instruction):
                setup[0] += 1
                instruction.then_inc(dve_setup, 1)
                dve.wait_ge(dve_setup, setup[0])

            dve.memset(bias_in[:], 0.0).then_inc(bias_cleared, 1)
            dve.memset(bias_parts[:].bitcast(F32), 0.0)
            dve.memset(ones[:].bitcast(F32), 1.0)

            def split(hi, lo, whole):
                then(dve.tensor_copy(hi, whole))
                return dve.tensor_tensor(lo, whole, hi.bitcast(F32), ALU.subtract)

            dve.wait_ge(score_weights_loaded, 4 * DMA)
            for c in range(C):
                for n in range(2):
                    then(dve.tensor_tensor_reduce(products[:], Wv_sb[:, c], aw_rows[:, n * D:(n + 1) * D],
                                                  1.0, 0.0, ALU.mult, ALU.add, u[:, c, n:n + 1]))
            for n in range(2):
                then(dve.tensor_tensor_reduce(products[:], bv_rows[:], aw_rows[:, n * D:(n + 1) * D],
                                              1.0, 0.0, ALU.mult, ALU.add, shift[:, n:n + 1]))
            then(dve.tensor_tensor(shift[:, 2:3], shift[:, 0:1], shift[:, 1:2], ALU.add))
            dve.tensor_scalar(shift[:, 3:4], shift[:, 2:3], ab_col[:, 0:1], 0.5, ALU.add,
                              ALU.mult).then_inc(shift_ready, 1)
            dve.wait_ge(Wk_loaded, HOPS * DMA)
            split(WY_hi[:, :, D:D + 2], WY_lo[:, :, D:D + 2], u[:])
            split(WY_hi[:, :, 0:D], WY_lo[:, :, 0:D], Wk_sb[:, 2]).then_inc(WY_ready, 1)
            for n in range(2):
                last = split(WX_hi[:, :, n], WX_lo[:, :, n], Wk_sb[:, n])
            then(last)
            dve.wait_ge(bias_loaded, 2 * DMA)
            for at in (0, 32):
                rows = slice(at, at + HOPS)
                then(dve.tensor_copy(bias_tmp[rows], bias_in[rows]))
            dve.tensor_copy(bias_parts[0:HOPS], bias_tmp[0:HOPS].bitcast(F32))
            dve.tensor_tensor(bias_parts[32:32 + HOPS], bias_in[32:32 + HOPS],
                              bias_tmp[32:32 + HOPS].bitcast(F32), ALU.subtract).then_inc(WX_ready, 1)

            def v1_lo(i, k):
                dve.wait_ge(v1_hi_ready, 2 * i + k + 1)
                dve.tensor_tensor(V1_lo[:], ps_x[:, :, D:2 * D], V1_hi[:].bitcast(F32),
                                  ALU.subtract).then_inc(v1_lo_ready, 1)

            def residual1(i, k):
                dve.wait_ge(h_done, 2 * i + k + 1)
                dve.wait_ge(nodes_loaded[k % 2], loads(i, k))
                dve.scalar_tensor_tensor(res1[:], ps_x[:, :, 0:D], 0.0, nodes_sb[k % 2][:],
                                         ALU.max, ALU.add).then_inc(res1_ready, 1)

            def leaky_sums(i, k):
                dve.wait_ge(sums_ready, 2 * i + k + 1)
                dve.scalar_tensor_tensor(leaky[:], sums[:], SLOPE, sums[:],
                                         ALU.mult, ALU.max).then_inc(leaky_ready, 1)

            def statistics1(i, k):
                dve.wait_ge(res1_ready, 2 * i + k + 1)
                for b in range(PER):
                    last = dve.bn_stats(stats1[:, b], res1[:, b])
                last.then_inc(stats1_ready, 1)

            def moments1_of(i, k):
                for b in range(PER):
                    last = dve.bn_aggr(moments1[:, b], stats1[:, b])
                last.then_inc(moments1_ready, 1)

            def aggregate_lo(i, k):
                dve.wait_ge(agg_hi_ready, 2 * i + k + 1)
                dve.tensor_tensor(agg_lo[:], ps_agg[:], agg_hi[:].bitcast(F32),
                                  ALU.subtract).then_inc(agg_lo_ready, 1)

            def transition(i, k):
                dve.wait_ge(exp_ready, 2 * i + k + 1)
                for b in range(PER):
                    last = dve.tensor_tensor_reduce(alpha[:, b], expd[:, b],
                                                    packed_sb[k % 2][:, AN + b * P:AN + (b + 1) * P],
                                                    1.0, 0.0, ALU.mult, ALU.add, rowsum[:, b:b + 1])
                last.then_inc(alpha_ready, 1)
                dve.wait_ge(alpha_ready, 2 * i + k + 1)
                dve.tensor_scalar(rowsum_eps[:], rowsum[:], ROWSUM_EPS, None, ALU.add).then_inc(rowsum_ready, 1)
                dve.wait_ge(rowsum_ready, 2 * i + k + 1)
                dve.reciprocal(inv_rowsum[:], rowsum_eps[:]).then_inc(inv_ready, 1)
                dve.wait_ge(inv_ready, 2 * i + k + 1)
                for b in range(PER):
                    last = dve.tensor_scalar(T[:, b], alpha[:, b], inv_rowsum[:, b:b + 1], None, ALU.mult)
                last.then_inc(t_ready, 1)

            def normalise2(i, k):
                dve.wait_ge(rstd2_ready, 2 * i + k + 1)
                if k >= 2:
                    dve.wait_ge(stored[k % 2], loads(i, k - 2))
                for b in range(PER):
                    last = dve.tensor_scalar(out_sb[k % 2][:, b], res2[:, b], moments2[:, b, 0:1],
                                             rstd2[:, b:b + 1], ALU.subtract, ALU.mult)
                last.then_inc(out_ready, 1)

            def v2_lo(i, k):
                dve.wait_ge(v2_hi_ready, 2 * i + k + 1)
                dve.tensor_tensor(V2_lo[:], ps_y[:, :, 0:D], V2_hi[:].bitcast(F32),
                                  ALU.subtract).then_inc(v2_lo_ready, 1)

            def normalise1(i, k):
                dve.wait_ge(rstd1_ready, 2 * i + k + 1)
                for b in range(PER):
                    last = dve.tensor_scalar(y[k % 2][:, b], res1[:, b], moments1[:, b, 0:1],
                                             rstd1[:, b:b + 1], ALU.subtract, ALU.mult)
                last.then_inc(y_ready, 1)

            def tt_lo(i, k):
                dve.wait_ge(tt_hi_ready, 2 * i + k + 1)
                dve.tensor_tensor(TT_lo[:], ps_t[:, 0:PER], TT_hi[:].bitcast(F32),
                                  ALU.subtract).then_inc(tt_lo_ready, 1)

            def residual2(i, k):
                if k > 0:
                    dve.wait_ge(out_ready, 2 * i + k)
                dve.wait_ge(out_done, 2 * i + k + 1)
                dve.tensor_tensor(res2[:], ps_out[:], y[k % 2][:], ALU.add).then_inc(res2_ready, 1)

            def statistics2(i, k):
                dve.wait_ge(res2_ready, 2 * i + k + 1)
                for b in range(PER):
                    last = dve.bn_stats(stats2[:, b], res2[:, b])
                last.then_inc(stats2_ready, 1)

            def moments2_of(i, k):
                for b in range(PER):
                    last = dve.bn_aggr(moments2[:, b], stats2[:, b])
                last.then_inc(moments2_ready, 1)

            def step(i, k):
                if there(i, k - 2):
                    dve.wait_ge(stats2_ready, 2 * i + k - 1)
                if there(i, k):
                    v1_lo(i, k)
                if there(i, k - 2):
                    moments2_of(i, k - 2)
                if there(i, k):
                    residual1(i, k)
                    statistics1(i, k)
                    dve.wait_ge(stats1_ready, 2 * i + k + 1)
                if there(i, k + 1):
                    leaky_sums(i, k + 1)
                if there(i, k):
                    moments1_of(i, k)
                if there(i, k - 1):
                    aggregate_lo(i, k - 1)
                if there(i, k + 1):
                    transition(i, k + 1)
                if there(i, k - 2):
                    normalise2(i, k - 2)
                if there(i, k + 1):
                    v2_lo(i, k + 1)
                if there(i, k):
                    normalise1(i, k)
                if there(i, k + 1):
                    tt_lo(i, k + 1)
                if there(i, k - 1):
                    residual2(i, k - 1)
                    statistics2(i, k - 1)
                if k == -2:
                    dve.wait_ge(w_loaded, DMA)
                    split(w_hi[:], w_lo[:], w_sb[:]).then_inc(w_ready, 1)

            all_steps(dve, step)

        @block.gpsimd
        def _(pool):
            pool.memset(identity[:], 0.0).then_inc(pool_setup, 1)
            pool.wait_ge(pool_setup, 1)
            pool.affine_select(out=identity[:], in_=identity[:], compare_op=ALU.not_equal, fill=1.0, base=0,
                               pattern=[[-1, P]], channel_multiplier=1).then_inc(identity_ready, 1)
            pool.memset(minus_half[:], -0.5).then_inc(pool_setup, 1)
            pool.memset(epsilon[:], NORM_EPS).then_inc(pool_setup, 1)
            pool.wait_ge(pool_setup, 3)

            def reciprocal_root(i, k, moments_ready, moments, var, var_ready, rstd, rstd_ready):
                pool.wait_ge(moments_ready, 2 * i + k + 1)
                pool.tensor_tensor(var[:], moments[:, :, 1], epsilon[:], ALU.add).then_inc(var_ready, 1)
                pool.wait_ge(var_ready, 2 * i + k + 1)
                pool.tensor_tensor(rstd[:], var[:], minus_half[:], ALU.pow).then_inc(rstd_ready, 1)

            def xt_lo(i, k):
                pool.wait_ge(xt_hi_ready, 2 * i + k + 1)
                pool.tensor_tensor(XT_lo[k % 2][:].rearrange("p c b i -> p (c b i)"),
                                   packed_sb[k % 2][:, XT:AN],
                                   XT_hi[k % 2][:].rearrange("p c b i -> p (c b i)").bitcast(F32),
                                   ALU.subtract).then_inc(xt_lo_ready, 1)

            def at_lo(i, k):
                pool.wait_ge(at_hi_ready, 2 * i + k + 1)
                pool.tensor_tensor(AT_lo[k % 2][:].rearrange("p b i -> p (b i)"),
                                   packed_sb[k % 2][:, AT:IN_COLS],
                                   AT_hi[k % 2][:].rearrange("p b i -> p (b i)").bitcast(F32),
                                   ALU.subtract).then_inc(at_lo_ready, 1)

            def y_lo_part(i, k):
                pool.wait_ge(y_hi_ready, 2 * i + k + 1)
                pool.tensor_tensor(y_lo[:], y[k % 2][:], y_hi[:].bitcast(F32),
                                   ALU.subtract).then_inc(y_lo_ready, 1)

            def step(i, k):
                if there(i, k):
                    reciprocal_root(i, k, moments1_ready, moments1, var1, var1_ready, rstd1, rstd1_ready)
                if there(i, k + 2):
                    xt_lo(i, k + 2)
                if there(i, k + 1):
                    at_lo(i, k + 1)
                if there(i, k):
                    y_lo_part(i, k)
                if there(i, k - 1):
                    reciprocal_root(i, k - 1, moments2_ready, moments2, var2, var2_ready, rstd2, rstd2_ready)

            all_steps(pool, step)

        @block.tensor
        def _(pe):
            def product(to, left, right, start, stop):
                terms = [(left[0], right[0]), (left[0], right[1]), (left[1], right[0])]
                for n, (a, b) in enumerate(terms):
                    last = pe.matmul(to, a, b, start=start and n == 0, stop=stop and n == 2,
                                     skip_group_check=True)
                return last

            def hop2_and_scores(i, k):
                pe.wait_ge(xt_lo_ready, 2 * i + k + 1)
                for b in range(PER):
                    for c in range(C):
                        last = product(ps_y[:, b, 0:D + 2], (XT_hi[k % 2][:, c, b], XT_lo[k % 2][:, c, b]),
                                       (WY_hi[:, c], WY_lo[:, c]), c == 0, c == C - 1)
                last.then_inc(y_done, 1)

            def hops01(i, k, b):
                if b == 0 and k > 0:
                    pe.wait_ge(res1_ready, 2 * i + k)
                for c in range(C):
                    product(ps_x[:, b], (XT_hi[k % 2][:, c, b], XT_lo[k % 2][:, c, b]),
                            (WX_hi[:, c].rearrange("p n d -> p (n d)"), WX_lo[:, c].rearrange("p n d -> p (n d)")),
                            c == 0, False)
                pe.matmul(ps_x[:, b, 0:D], ones[:], bias_parts[:], start=False, stop=False,
                          skip_group_check=True)

            def spread_scores(i, k):
                pe.wait_ge(scores_ready, 2 * i + k + 1)
                for b in range(PER):
                    last = pe.transpose(ps_s[:, b], scores[:, b, 0:1].broadcast_to([P, P]), identity[:])
                last.then_inc(spread_done, 1)

            def transpose_t(i, k):
                pe.wait_ge(t_ready, 2 * i + k + 1)
                for b in range(PER):
                    last = pe.transpose(ps_t[:, b], T[:, b], identity[:])
                last.then_inc(tt_done, 1)

            def propagate_v2(i, k):
                pe.wait_ge(v2_lo_ready, 2 * i + k + 1)
                pe.wait_ge(tt_lo_ready, 2 * i + k + 1)
                for b in range(PER):
                    last = product(ps_x[:, b, D:2 * D], (TT_hi[:, b], TT_lo[:, b]),
                                   (V2_hi[:, b], V2_lo[:, b]), False, False)
                last.then_inc(v1_done, 1)

            def propagate_v1(i, k):
                pe.wait_ge(v1_lo_ready, 2 * i + k + 1)
                for b in range(PER):
                    last = product(ps_x[:, b, 0:D], (TT_hi[:, b], TT_lo[:, b]),
                                   (V1_hi[:, b], V1_lo[:, b]), False, True)
                last.then_inc(h_done, 1)

            def aggregate(i, k):
                pe.wait_ge(y_lo_ready, 2 * i + k + 1)
                pe.wait_ge(at_lo_ready, 2 * i + k + 1)
                for c in range(C):
                    for b in range(PER):
                        cols = slice(c * P, (c + 1) * P)
                        last = product(ps_agg[:, c, b], (y_hi[:, b, cols], y_lo[:, b, cols]),
                                       (AT_hi[k % 2][:, b], AT_lo[k % 2][:, b]), True, True)
                last.then_inc(agg_done, 1)

            def project(i, k):
                pe.wait_ge(agg_lo_ready, 2 * i + k + 1)
                if k > 0:
                    pe.wait_ge(res2_ready, 2 * i + k)
                for b in range(PER):
                    for c in range(C):
                        last = product(ps_out[:, b], (agg_hi[:, c, b], agg_lo[:, c, b]),
                                       (w_hi[:, c], w_lo[:, c]), c == 0, c == C - 1)
                last.then_inc(out_done, 1)

            def step(i, k):
                if there(i, k):
                    propagate_v2(i, k)
                if there(i, k + 1):
                    if k == -1:
                        pe.wait_ge(WY_ready, 1)
                    hop2_and_scores(i, k + 1)
                if there(i, k):
                    propagate_v1(i, k)
                if there(i, k + 1):
                    if k == -1:
                        pe.wait_ge(identity_ready, 1)
                    spread_scores(i, k + 1)
                if there(i, k - 1):
                    if k == 1:
                        pe.wait_ge(w_ready, 1)
                    aggregate(i, k - 1)
                if there(i, k + 1):
                    if k == -1:
                        pe.wait_ge(WX_ready, 1)
                    hops01(i, k + 1, 0)
                if there(i, k - 1):
                    project(i, k - 1)
                if there(i, k + 1):
                    transpose_t(i, k + 1)
                    hops01(i, k + 1, 1)

            all_steps(pe, step)


def kernel(**inputs):
    import numpy as np
    import concourse.bacc as bacc
    from concourse.bass_utils import run_bass_kernel_spmd

    x = np.asarray(inputs["x"])
    adj = np.asarray(inputs["adj"])
    graphs, n, d = x.shape
    pairs = graphs // PER
    xt = x.reshape(pairs, PER, n, d // P, P).transpose(0, 4, 3, 1, 2).reshape(pairs, P, PER * d)
    a = adj.reshape(pairs, PER, n, n)
    packed = np.ascontiguousarray(np.concatenate(
        [xt, a.transpose(0, 2, 1, 3).reshape(pairs, n, PER * n),
         a.transpose(0, 3, 1, 2).reshape(pairs, n, PER * n)], axis=2))
    nodes = np.ascontiguousarray(x.reshape(pairs, PER, n, d).transpose(0, 2, 1, 3).reshape(pairs, n, PER * d))
    arrays = {"packed": packed, "nodes": nodes}
    for name in ("Wv", "bv", "aw", "ab", "Wk", "bk"):
        arrays[name] = np.ascontiguousarray(inputs["L0_gnn_" + name])
    arrays["aw"] = arrays["aw"].reshape(-1)
    arrays["w"] = np.ascontiguousarray(inputs["L1_gnn_w"])

    nc = bacc.Bacc("TRN2", target_bir_lowering=False, num_devices=1)
    args = {k: nc.dram_tensor(f"{k}_dram", v.shape, mybir.dt.from_np(v.dtype), kind="ExternalInput").ap()
            for k, v in arrays.items()}
    out = nc.dram_tensor("out_dram", (pairs, n, PER * d), F32, kind="ExternalOutput").ap()
    resnorm_graph_kernel(nc, **args, out=out)
    r = run_bass_kernel_spmd(nc, [{f"{k}_dram": v for k, v in arrays.items()}], core_ids=[0])
    got = np.asarray(r.results[0]["out_dram"])
    return got.reshape(pairs, n, PER, d).transpose(0, 2, 1, 3).reshape(graphs, n, d)
```
